# Optimizing a Trainium2 kernel written in Bass

```python
import numpy as np
import jax
import jax.numpy as jnp

def _softmax(x, axis=-1):
    return jax.nn.softmax(x, axis=axis)

def _gelu(x):
    return jax.nn.gelu(x, approximate=True)

def _silu(x):
    return jax.nn.silu(x)

def _sigmoid(x):
    return jax.nn.sigmoid(x)

def _layernorm(x, axis=-1, eps=1e-05):
    m = jnp.mean(x, axis=axis, keepdims=True)
    v = jnp.var(x, axis=axis, keepdims=True)
    return (x - m) / jnp.sqrt(v + eps)

def _scatter_add(tgt, idx, src, axis=0):
    return tgt.at[idx].add(src)

def _segment_sum(src, seg, n):
    return jax.ops.segment_sum(src, seg, n)
kernel_name = 'mk_cond_resid_d2_seqx_r4_2a4fdc'

def setup_inputs(seed: int=0):
    np.random.seed(seed)
    _w = jnp.asarray

    def _rec_inputs():
        import jax
        import jax.numpy as jnp
        _rk = jax.random.key(seed)
        x = 7.22e-05 + 1 * jax.random.normal(jax.random.fold_in(_rk, 1), (2, 1024, 256), jnp.float32)
        _lenS = 1024 - jax.random.randint(jax.random.fold_in(_rk, 7), (2,), 0, max(1, 1024 // 4) + 1, jnp.int32)
        _lenS2 = 1024 - jax.random.randint(jax.random.fold_in(_rk, 8), (2,), 0, max(1, 1024 // 4) + 1, jnp.int32)
        itok_B_0_2 = jax.random.randint(jax.random.fold_in(_rk, 11), (2,), 0, 3, jnp.int32)
        itok_B_0_15 = jax.random.randint(jax.random.fold_in(_rk, 12), (2,), 0, 16, jnp.int32)
        return (x, itok_B_0_2, itok_B_0_15)
    x, itok_B_0_2, itok_B_0_15 = _rec_inputs()

    def _L0_cond_setup():
        import jax, jax.numpy as jnp
        import numpy as np
        B, S, D, F, E = (8, 256, 256, 1024, 4)

        def _dense(x, wi, wo):
            return jax.nn.relu(x @ wi) @ wo
        key = jax.random.key(seed)
        ks = jax.random.split(key, 10)
        scale = 0.02
        return {'hidden_states': jax.random.normal(ks[0], (B, S, D), jnp.float32), 'type_idx': jax.random.randint(ks[1], (B,), 0, 3, jnp.int32), 'expert_wi': jax.random.normal(ks[2], (E, D, F), jnp.float32) * scale, 'expert_wo': jax.random.normal(ks[3], (E, F, D), jnp.float32) * scale, 'share_wi': jax.random.normal(ks[4], (3, D, F), jnp.float32) * scale, 'share_wo': jax.random.normal(ks[5], (3, F, D), jnp.float32) * scale, 'gate_vecs': jnp.array([[0.22, 0.22, 0.2, 0.2], [0.2, 0.22, 0.22, 0.2], [0.2, 0.2, 0.22, 0.22]], jnp.float32), 'gate_w1': jax.random.normal(ks[6], (4 * D, D), jnp.float32) * scale, 'gate_w2': jax.random.normal(ks[7], (D, 4), jnp.float32) * scale}
    _L0_cond_all = _L0_cond_setup()
    _L0_cond_in = {k: v for k, v in _L0_cond_all.items() if k in ('expert_wi', 'expert_wo', 'share_wi', 'share_wo', 'gate_vecs', 'gate_w1', 'gate_w2')}
    del _L0_cond_all

    def _L1_cond_setup():
        import jax, jax.numpy as jnp
        import numpy as np
        B, N, DIM = (32, 256, 256)
        HID = 1024
        PART = 64
        OUT = 256
        SHARED = OUT - PART
        E = 16
        key = jax.random.key(seed)
        ks = jax.random.split(key, 8)
        s = 0.02
        return {'x': jax.random.normal(ks[0], (B, N, DIM), dtype=jnp.float32), 'indices': jax.random.randint(ks[1], (B,), 0, E, dtype=jnp.int64), 'fc1_w': jax.random.normal(ks[2], (HID, DIM), dtype=jnp.float32) * s, 'fc1_b': jnp.zeros((HID,), dtype=jnp.float32), 'fc2_w': jax.random.normal(ks[3], (SHARED, HID), dtype=jnp.float32) * s, 'fc2_b': jnp.zeros((SHARED,), dtype=jnp.float32), 'experts_w': jax.random.normal(ks[4], (E, PART, HID), dtype=jnp.float32) * s, 'experts_b': jnp.zeros((E, PART), dtype=jnp.float32)}
    _L1_cond_all = _L1_cond_setup()
    _L1_cond_in = {k: v for k, v in _L1_cond_all.items() if k in ('fc1_w', 'fc1_b', 'fc2_w', 'fc2_b', 'experts_w', 'experts_b')}
    del _L1_cond_all
    return {'x': x, 'itok_B_0_2': itok_B_0_2, 'itok_B_0_15': itok_B_0_15, 'L0_cond_expert_wi': _L0_cond_in['expert_wi'], 'L0_cond_expert_wo': _L0_cond_in['expert_wo'], 'L0_cond_share_wi': _L0_cond_in['share_wi'], 'L0_cond_share_wo': _L0_cond_in['share_wo'], 'L0_cond_gate_vecs': _L0_cond_in['gate_vecs'], 'L0_cond_gate_w1': _L0_cond_in['gate_w1'], 'L0_cond_gate_w2': _L0_cond_in['gate_w2'], 'L1_cond_fc1_w': _L1_cond_in['fc1_w'], 'L1_cond_fc1_b': _L1_cond_in['fc1_b'], 'L1_cond_fc2_w': _L1_cond_in['fc2_w'], 'L1_cond_fc2_b': _L1_cond_in['fc2_b'], 'L1_cond_experts_w': _L1_cond_in['experts_w'], 'L1_cond_experts_b': _L1_cond_in['experts_b']}

def reference(x, itok_B_0_2, itok_B_0_15, L0_cond_expert_wi, L0_cond_expert_wo, L0_cond_share_wi, L0_cond_share_wo, L0_cond_gate_vecs, L0_cond_gate_w1, L0_cond_gate_w2, L1_cond_fc1_w, L1_cond_fc1_b, L1_cond_fc2_w, L1_cond_fc2_b, L1_cond_experts_w, L1_cond_experts_b):
    import jax
    import jax.numpy as jnp

    def _L0_cond_ref(hidden_states, type_idx, expert_wi, expert_wo, share_wi, share_wo, gate_vecs, gate_w1, gate_w2):
        import jax, jax.numpy as jnp
        import numpy as np
        B, S, D, F, E = (8, 256, 256, 1024, 4)

        def _dense(x, wi, wo):
            return jax.nn.relu(x @ wi) @ wo
        s0 = _dense(hidden_states, share_wi[0], share_wo[0])
        s1 = _dense(hidden_states, share_wi[1], share_wo[1])
        s2 = _dense(hidden_states, share_wi[2], share_wo[2])
        idx_a = type_idx
        idx_b = type_idx + 1
        out_a = jnp.einsum('bsf,bfd->bsd', jax.nn.relu(jnp.einsum('bsd,bdf->bsf', hidden_states, expert_wi[idx_a])), expert_wo[idx_a])
        out_b = jnp.einsum('bsf,bfd->bsd', jax.nn.relu(jnp.einsum('bsd,bdf->bsf', hidden_states, expert_wi[idx_b])), expert_wo[idx_b])
        p = jax.nn.softmax(gate_vecs / 0.1, axis=-1)
        wa = p[type_idx, idx_a][:, None, None]
        wb = p[type_idx, idx_b][:, None, None]
        expert_out = out_a * wa + out_b * wb
        gi = jnp.concatenate([expert_out[:, 0], s0[:, 0], s1[:, 0], s2[:, 0]], axis=-1)
        g = jax.nn.softmax(jax.nn.relu(gi @ gate_w1) @ gate_w2, axis=-1)
        out = expert_out * g[:, 0, None, None] + s0 * g[:, 1, None, None] + s1 * g[:, 2, None, None] + s2 * g[:, 3, None, None]
        return out

    def _L1_cond_ref(x, indices, fc1_w, fc1_b, fc2_w, fc2_b, experts_w, experts_b):
        import jax, jax.numpy as jnp
        import numpy as np
        B, N, DIM = (32, 256, 256)
        HID = 1024
        PART = 64
        OUT = 256
        SHARED = OUT - PART
        E = 16
        h = jax.nn.gelu(jnp.einsum('bnd,hd->bnh', x, fc1_w) + fc1_b, approximate=False)
        shared = jnp.einsum('bnh,sh->bns', h, fc2_w) + fc2_b
        We = experts_w[indices]
        be = experts_b[indices]
        expert_x = jnp.einsum('bnh,bph->bnp', h, We) + be[:, None, :]
        return jnp.concatenate([shared, expert_x], axis=-1)
    x = x + _L0_cond_ref(x, itok_B_0_2, L0_cond_expert_wi, L0_cond_expert_wo, L0_cond_share_wi, L0_cond_share_wo, L0_cond_gate_vecs, L0_cond_gate_w1, L0_cond_gate_w2)
    x = x + _L1_cond_ref(x, itok_B_0_15, L1_cond_fc1_w, L1_cond_fc1_b, L1_cond_fc2_w, L1_cond_fc2_b, L1_cond_experts_w, L1_cond_experts_b)
    return x

_drawn_inputs = setup_inputs


def setup_inputs(seed=0):
    import zlib

    import numpy as np

    out = dict(_drawn_inputs(seed))
    spreads = {'L1_cond_fc1_b': (0.0, 0.1), 'L1_cond_fc2_b': (0.0, 0.1), 'L1_cond_experts_b': (0.0, 0.1)}
    factors = {'L0_cond_expert_wi': 4.935,
     'L0_cond_expert_wo': 4.095,
     'L0_cond_gate_vecs': 8.0,
     'L0_cond_gate_w1': 8.0,
     'L0_cond_gate_w2': 8.0}
    for name, (base, spread) in spreads.items():
        noise = np.random.default_rng([zlib.crc32(name.encode()), seed]).standard_normal(out[name].shape)
        drawn = base * np.exp(spread * noise) if base else spread * noise
        out[name] = jnp.asarray(drawn.astype(out[name].dtype))
    for name, factor in factors.items():
        out[name] = (out[name] * factor).astype(out[name].dtype)
    return out
```

```python
import concourse.bass as bass
from concourse import mybir
from contextlib import ExitStack


def residual_moe_program(nc, x, itok_gate, itok_part, expert_wi, expert_wo, share_wi, share_wo, gate_vecs,
                         gate_w1, gate_w2, fc1_w, fc1_b, fc2_w, fc2_b, experts_w, experts_b, out):
    f32 = mybir.dt.float32
    f32r = mybir.dt.float32r
    i32 = mybir.dt.int32
    ALU = mybir.AluOpType
    ACT = mybir.ActivationFunctionType
    AX = mybir.AxisListType

    P = 128
    B, S, D = x.shape
    F = share_wi.shape[2]
    SHARED = fc2_w.shape[0]
    NSH = share_wi.shape[0]
    NE = expert_wi.shape[0]
    NPART = experts_w.shape[0]
    T = 512
    NT = B * S // T
    TB = S // T
    DK = D // P
    NF = F // P
    WC = DK * P + D
    RING = 4
    PARTS = 4
    REST = SHARED - P

    U_A = NSH * NT
    U_B = U_A + NT
    U_L1 = U_B + NT
    NU = U_L1 + NT

    def first_unit(m):
        return m * NT if m <= NSH else U_A + (m - NSH) * TB

    M_A, M_B, M_L1 = NSH, NSH + B, NSH + 2 * B

    x_nat_dram = x.rearrange("b (n p) d -> p (b n) d", p=P)
    out_dram = out.rearrange("b (n p) d -> p (b n) d", p=P)

    ctx = ExitStack()
    with ctx:
        def sb(name, shape, dt=f32):
            return ctx.enter_context(nc.sbuf_tensor(name, shape, dt))

        def sem(name):
            return ctx.enter_context(nc.semaphore(name))

        w_hi = sb("w_hi", [P, NF, WC], f32r)
        w_lo = sb("w_lo", [P, NF, WC], f32r)
        stage = sb("stage", [P, 2, NF, WC])
        x_hi = sb("x_hi", [P, NT, DK, T], f32r)
        x_lo = sb("x_lo", [P, NT, DK, T], f32r)
        hid_hi = sb("hid_hi", [P, RING, T], f32r)
        hid_lo = sb("hid_lo", [P, RING, T], f32r)
        gelu = sb("gelu", [P, 2, T])
        share_out = sb("share_out", [P, NSH, NT, DK, T])
        mix = sb("mix", [P, NT, DK * T])
        gw1 = sb("gw1", [P, (1 + NSH) * DK, D])
        gw2 = sb("gw2", [P, DK, 4])
        ident = sb("ident", [P, P])
        zeros = sb("zeros", [P, P])
        ones = sb("ones", [P, 1])
        gate_part = sb("gate_part", [P, D])
        gate_hid = sb("gate_hid", [P, DK, P])
        idx = sb("idx", [1, 2 * B], i32)
        b1 = sb("b1", [P, NF])
        b2 = sb("b2", [P, B, DK])
        gv = sb("gv", [P, B, 6])
        pair_max = sb("pair_max", [P, B])
        pair_bias = sb("pair_bias", [P, B])
        pair_exp = sb("pair_exp", [P, B, 6])
        pair_sum = sb("pair_sum", [P, B])
        pair_inv = sb("pair_inv", [P, B])
        pair_w = sb("pair_w", [P, B, 2])
        gate_max = sb("gate_max", [P, B])
        gate_bias = sb("gate_bias", [P, B])
        gate_exp = sb("gate_exp", [P, B, 4])
        gate_sum = sb("gate_sum", [P, B])
        gate_inv = sb("gate_inv", [P, B])
        gate = sb("gate", [P, B, 4])

        mix_v = mix[:, :, :].rearrange("p t (k n) -> p t k n", k=DK)
        nat_v = mix[:, :, :].rearrange("p t (j d) -> p t j d", d=D)

        def bank(name):
            return ctx.enter_context(nc.psum_tensor(name, [P, T], f32))

        hid_ps = [bank(f"hid_ps{i}") for i in range(2)]
        out_ps = [[bank(f"out_ps{i}{k}") for k in range(DK)] for i in range(2)]
        turn_ps = bank("turn_ps")

        x_loaded = [sem(f"x_loaded{t}") for t in range(NT)]
        part_loaded = [sem(f"part_loaded{i}") for i in range(PARTS)]
        set_loaded = sem("set_loaded")
        l1_loaded = sem("l1_loaded")
        rows_loaded = sem("rows_loaded")
        idx_loaded = sem("idx_loaded")
        gv_loaded = sem("gv_loaded")
        gw_loaded = sem("gw_loaded")
        bias_loaded = sem("bias_loaded")
        out_stored = sem("out_stored")
        zeros_made = sem("zeros_made")
        ident_made = sem("ident_made")
        x_turned = sem("x_turned")
        x_hi_done = sem("x_hi_done")
        x_ready = sem("x_ready")
        up_done = sem("up_done")
        hi_done = sem("hi_done")
        gelu_done = sem("gelu_done")
        gelu_hi = sem("gelu_hi")
        hid_ready = sem("hid_ready")
        down_done = sem("down_done")
        w_turned = sem("w_turned")
        w_hi_done = sem("w_hi_done")
        w_ready = sem("w_ready")
        out_taken = sem("out_taken")
        pair_step = sem("pair_step")
        pair_exp_done = sem("pair_exp_done")
        gate_sums = sem("gate_sums")
        gate_up = sem("gate_up")
        last_half = sem("last_half")
        last_taken = sem("last_taken")
        gate_hid_done = sem("gate_hid_done")
        gate_logits = sem("gate_logits")
        gate_step = sem("gate_step")
        gate_exp_done = sem("gate_exp_done")
        mix_step = sem("mix_step")
        x1_hi_done = sem("x1_hi_done")
        x1_split = sem("x1_split")
        y_turned = sem("y_turned")
        y_rows = sem("y_rows")

        block = ctx.enter_context(nc.Block())

        def set_of(u):
            return u // NT if u < U_A else (M_A + (u - U_A) // TB if u < U_L1 else M_L1)

        SPLITS = {first_unit(m) - 1: m for m in range(1, M_L1 + 1)}
        ROWS_UNIT = U_L1 + TB - 1
        SPLITS[ROWS_UNIT] = M_L1 + 1
        GATE_UNITS = {U_B + TB * b + 1: b for b in range(B)}
        Y_STEPS = {(U_L1 + 2, 1 + n): n for n in range(4)}
        Y_STEPS.update({(U_L1 + 3, 1): 4, (U_L1 + 3, 2): 5})

        HALVES = NT * DK
        mix_ops = []
        for h in range(HALVES):
            mix_ops += [("sum", h, k) for k in range(2)]
            if h:
                mix_ops.append(("lo", h - 1, 0))
            mix_ops += [("sum", h, k) for k in range(2, 5)]
        mix_ops.append(("lo", HALVES - 1, 0))
        mix_at = {op: n for n, op in enumerate(mix_ops)}
        MIX_RATE = {U_B + 2: 2, U_B + 3: 1, U_L1: 2, U_L1 + 1: 1}
        mix_plan, planned = {}, 0
        for u, rate in MIX_RATE.items():
            for f in range(NF):
                mix_plan[u, f] = range(planned, planned + rate)
                planned += rate
        assert planned == len(mix_ops)

        GATE_TERMS = (1 + NSH) * DK
        gate_plan = {}
        for u, b in GATE_UNITS.items():
            for n in range(DK, GATE_TERMS):
                gate_plan[u - 1, n - DK] = (b, n)
            for n in range(DK):
                gate_plan[u, n] = (b, n)
        gate_order = list(range(DK, GATE_TERMS)) + list(range(DK))
        WARM = 7
        WARM_BETWEEN = 3
        GATE_STEPS = 5
        mix_sums = [sum(kind == "sum" for kind, _, _ in mix_ops[:n]) for n in range(len(mix_ops))]

        def y_bank(n):
            return hid_ps[0] if n == 2 * NT - 1 else turn_ps

        class Place:

            def __init__(self, i, unit, chunk, wset):
                self.i, self.tile, self.unit, self.chunk, self.set = i, i % NT, unit, chunk, wset

        def fixed(u):
            return Place(u, u, NF * u, NF * set_of(u))

        def shared_loop(eng):
            with eng.Fori(1, NSH) as m:
                units = eng.snap(m * NT)
                chunks = eng.snap(m * (NT * NF))
                sets = eng.snap(m * NF)
                for t in range(NT):
                    yield m, Place(NT + t, units + t, chunks + NF * t, sets)

        @block.sync
        def _(sp):
            def load_set(i, wi, wo, fs, loaded):
                cols = slice(fs.start * P, fs.stop * P)
                for k in range(DK):
                    sp.dma_start(stage[:, i, fs, k * P:(k + 1) * P],
                                 wi[k * P:(k + 1) * P, cols].rearrange("p (f c) -> p f c", c=P))\
                        .then_inc(loaded, 16)
                sp.dma_start(stage[:, i, fs, DK * P:WC], wo[cols, :].rearrange("(f p) d -> p f d", p=P))\
                    .then_inc(loaded, 16)

            sp.dma_start(nat_v[:, 0, :, :], x_nat_dram[:, 0:4, :]).then_inc(x_loaded[0], 16)
            step = NF // PARTS
            for n in range(PARTS):
                load_set(0, share_wi[0], share_wo[0], slice(n * step, (n + 1) * step), part_loaded[n])
            for t in range(1, NT):
                sp.dma_start(nat_v[:, t, :, :], x_nat_dram[:, 4 * t:4 * t + 4, :]).then_inc(x_loaded[t], 16)
            whole = slice(0, NF)
            load_set(1, share_wi[1], share_wo[1], whole, set_loaded)

            sp.dma_start(idx[0:1, 0:B], itok_gate.rearrange("(a n) -> a n", a=1)).then_inc(idx_loaded, 16)
            sp.dma_start(idx[0:1, B:2 * B], itok_part.rearrange("(a n) -> a n", a=1)).then_inc(idx_loaded, 16)
            sp.dma_start(gw1[:, :, :], gate_w1.rearrange("(n p) d -> p n d", p=P)).then_inc(gw_loaded, 16)
            sp.dma_start(gw2[:, :, :], gate_w2.rearrange("(n p) d -> p n d", p=P)).then_inc(gw_loaded, 16)
            sp.wait_ge(idx_loaded, 32)
            t_idx = [sp.value_load(idx[0:1, b:b + 1], min_val=0, max_val=NE - 2) for b in range(B)]
            e_idx = [sp.value_load(idx[0:1, B + b:B + b + 1], min_val=0, max_val=NPART - 1) for b in range(B)]
            gv_flat = gate_vecs.rearrange("a c -> (a c)")
            col = lambda v: v.rearrange("(p a) -> p a", a=1)
            with nc.allow_non_contiguous_dma(reason="biases, one element a partition"):
                sp.dma_start(b1[:, :], fc1_b.rearrange("(f p) -> p f", p=P)).then_inc(bias_loaded, 16)
                for b in range(B):
                    row = gate_vecs[bass.ds(t_idx[b], 1), :].rearrange("a c -> (a c)")
                    sp.dma_start(gv[:, b, 0:4], row.partition_broadcast(P)).then_inc(gv_loaded, 16)
                    sp.dma_start(gv[:, b, 4:6], gv_flat[bass.ds(t_idx[b] * (NE + 1), 2)].partition_broadcast(P))\
                        .then_inc(gv_loaded, 16)
                    sp.dma_start(b2[:, b, 0:1], col(fc2_b[0:P])).then_inc(bias_loaded, 16)
                    sp.dma_start(b2[0:REST, b, 1:2], col(fc2_b[P:SHARED])).then_inc(bias_loaded, 16)
                    sp.dma_start(b2[REST:P, b, 1:2], experts_b[bass.ds(e_idx[b], 1), :].rearrange("a p -> p a"))\
                        .then_inc(bias_loaded, 16)

            for m in range(2, M_L1):
                sp.wait_ge(w_ready, NF * (m - 1))
                sp.wait_ge(set_loaded, 48 * (m - 1))
                if m < M_A:
                    load_set(m % 2, share_wi[m], share_wo[m], whole, set_loaded)
                else:
                    e, b = (m - M_A) // B, (m - M_A) % B
                    at = bass.ds(t_idx[b] + e, 1)
                    load_set(m % 2, expert_wi[at, :, :].rearrange("a d f -> (a d) f"),
                             expert_wo[at, :, :].rearrange("a f d -> (a f) d"), whole, set_loaded)

            def load_rows(b, loaded):
                dst = stage[:, M_L1 % 2, :, WC - P:WC]
                sp.dma_start(dst[0:REST], fc2_w[P:SHARED, :].rearrange("p (f c) -> p f c", c=P))\
                    .then_inc(loaded, 16)
                sp.dma_start(dst[REST:P], experts_w[bass.ds(e_idx[b], 1), :, :]
                             .rearrange("a p (f c) -> (a p) f c", c=P)).then_inc(loaded, 16)

            dst = stage[:, M_L1 % 2, :, :]
            sp.wait_ge(w_ready, NF * (M_L1 - 1))
            sp.dma_start(dst[:, :, 0:DK * P], fc1_w.rearrange("(f p) d -> p f d", p=P)).then_inc(l1_loaded, 16)
            sp.dma_start(dst[:, :, DK * P:WC - P], fc2_w[0:P, :].rearrange("p (f c) -> p f c", c=P))\
                .then_inc(l1_loaded, 16)
            load_rows(0, l1_loaded)
            sp.wait_ge(w_ready, NF * (M_L1 + 1))
            load_rows(1, rows_loaded)

            for n in range(2 * NT):
                t, cols = n // DK, slice(n % DK * P, (n % DK + 1) * P)
                sp.wait_ge(y_rows, n + 1)
                sp.dma_start(out_dram[:, 4 * t:4 * t + 4, cols], nat_v[:, t, :, cols]).then_inc(out_stored, 16)
            sp.wait_ge(out_stored, 16 * 2 * NT)

        @block.gpsimd
        def _(pool):
            pool.memset(zeros[:, :], 0.0).then_inc(zeros_made, 1)
            pool.memset(ones[:, :], 1.0).then_inc(ident_made, 1)
            pool.memset(ident[:, :], 0.0).then_inc(ident_made, 1)
            pool.wait_ge(ident_made, 2)
            pool.affine_select(out=ident[:, :], in_=ident[:, :], compare_op=ALU.not_equal, fill=1.0, base=0,
                               pattern=[[-1, P]], channel_multiplier=1).then_inc(ident_made, 1)

        @block.tensor
        def _(pe):
            def product(ps, hi_w, lo_w, hi_m, lo_m, start, stop):
                pe.matmul(ps, hi_w, hi_m, start=start, stop=False)
                pe.matmul(ps, hi_w, lo_m, start=False, stop=False)
                return pe.matmul(ps, lo_w, hi_m, start=False, stop=stop)

            def up(tile, f):
                for k in range(DK):
                    cols = slice(k * P, (k + 1) * P)
                    mm = product(hid_ps[f % 2][:, :], w_hi[:, f, cols], w_lo[:, f, cols],
                                 x_hi[:, tile, k, :], x_lo[:, tile, k, :], k == 0, k == DK - 1)
                mm.then_inc(up_done, 1)

            def down(parity, f, last=False):
                for k in range(DK):
                    cols = slice((DK + k) * P, (DK + k + 1) * P)
                    mm = product(out_ps[parity][k][:, :], w_hi[:, f, cols], w_lo[:, f, cols],
                                 hid_hi[:, f % RING, :], hid_lo[:, f % RING, :], f == 0, f == NF - 1)
                    if last and k == 0:
                        mm.then_inc(last_half, 1)
                mm.then_inc(down_done, 1)

            def turn_x(n):
                t, k = n // DK, n % DK
                dst = out_ps[1][k] if t == 0 else turn_ps
                if k == 0:
                    pe.wait_ge(x_loaded[t], 16)
                if n > DK:
                    pe.wait_ge(x_ready, n)
                for j in range(T // P):
                    mm = pe.transpose(dst[:, j * P:(j + 1) * P], nat_v[:, t, j, k * P:(k + 1) * P], ident[:, :])
                mm.then_inc(x_turned, 1)

            def turn_weights(f):
                if f == 0:
                    pe.wait_ge(l1_loaded, 64)
                else:
                    pe.wait_ge(w_ready, NF * M_L1 + f)
                for j in range(WC // P):
                    cols = slice(j * P, (j + 1) * P)
                    mm = pe.transpose(turn_ps[:, cols], stage[:, M_L1 % 2, f, cols], ident[:, :])
                mm.then_inc(w_turned, 1)

            def turn_rows(f):
                if f == 0:
                    pe.wait_ge(rows_loaded, 32)
                pe.wait_ge(w_ready, NF * (M_L1 + 1) + f)
                pe.transpose(turn_ps[:, 0:P], stage[:, M_L1 % 2, f, WC - P:WC], ident[:, :]).then_inc(w_turned, 1)

            def turn_y(n):
                t, k = n // DK, n % DK
                if n == 2 * NT - 2:
                    pe.wait_ge(last_taken, 1)
                else:
                    pe.wait_ge(out_taken, U_L1 + t + 1)
                if n == 0:
                    pe.wait_ge(w_ready, NF * (M_L1 + 2))
                elif n < 2 * NT - 1:
                    pe.wait_ge(y_rows, n)
                for j in range(T // P):
                    cols = slice(j * P, (j + 1) * P)
                    mm = pe.transpose(y_bank(n)[:, cols], share_out[:, 0, t, k, cols], ident[:, :])
                mm.then_inc(y_turned, 1)

            def gate_first(b):
                pe.wait_ge(out_taken, U_B + TB * b + 1)
                pe.wait_ge(gate_sums, GATE_TERMS * (b + 1))
                for half in range(DK):
                    mm = pe.matmul(out_ps[0][0][:, half:half + 1], gate_part[:, half * P:(half + 1) * P],
                                   ones[:, :], start=True, stop=True)
                mm.then_inc(gate_up, 1)

            def gate_second(b):
                if b == 0:
                    pe.wait_ge(gw_loaded, 32)
                pe.wait_ge(gate_hid_done, b + 1)
                for half in range(DK):
                    mm = pe.matmul(out_ps[0][1][:, 0:4], gate_hid[:, half, :], gw2[:, half, :],
                                   start=(half == 0), stop=(half == DK - 1))
                mm.then_inc(gate_logits, 1)

            def unit(at):
                u = at.i
                for f in range(NF):
                    pe.wait_ge(hid_ready, at.chunk + (f + 1))
                    if f + 2 < NF:
                        if u == first_unit(set_of(u)):
                            pe.wait_ge(w_ready, at.set + (f + 3))
                        up(at.tile, f + 2)
                    elif u + 1 < NU:
                        if u + 1 == first_unit(set_of(u + 1)):
                            pe.wait_ge(w_ready, at.set + (f + 3))
                        if f + 2 == NF and u + 1 < NT:
                            pe.wait_ge(x_ready, DK * (u + 2))
                        if f + 2 == NF and u + 1 >= U_L1:
                            pe.wait_ge(x1_split, DK * (u + 2 - U_L1))
                        up((at.tile + 1) % NT, f + 2 - NF)
                    if f == 0 and u >= 2:
                        pe.wait_ge(out_taken, at.unit + (-1))
                    if f == 0 and u in (U_B + 2, U_L1):
                        pe.wait_ge(gate_exp_done, (u - U_B) // 2)
                    if u == ROWS_UNIT + 1:
                        pe.wait_ge(w_ready, NF * (M_L1 + 1) + f + 1)
                    down(u % 2, f, last=(u == NU - 1 and f == NF - 1))
                    if u == 0 and f + DK < HALVES:
                        turn_x(f + DK)
                    if SPLITS.get(u) == M_L1:
                        turn_weights(f)
                    if SPLITS.get(u) == M_L1 + 1:
                        turn_rows(f)
                    if u in GATE_UNITS and f == 2:
                        gate_first(GATE_UNITS[u])
                    if u in GATE_UNITS and f == 4:
                        gate_second(GATE_UNITS[u])
                    if (u, f) in Y_STEPS:
                        turn_y(Y_STEPS[u, f])

            def warm(n):
                for _ in range(n):
                    pe.matmul(out_ps[0][0][:, 0:P], zeros[:, :], zeros[:, :], start=True, stop=True)

            def first_up():
                ps = hid_ps[0][:, :]
                for k in range(DK):
                    hi_w, lo_w = (w[:, 0, k * P:(k + 1) * P] for w in (w_hi, w_lo))
                    pe.wait_ge(x_hi_done, k + 1)
                    if k == 0:
                        pe.wait_ge(w_hi_done, 1)
                    pe.matmul(ps, hi_w, x_hi[:, 0, k, :], start=(k == 0), stop=False)
                    pe.wait_ge(x_ready, k + 1)
                    pe.matmul(ps, hi_w, x_lo[:, 0, k, :], start=False, stop=False)
                    if k == 0:
                        pe.wait_ge(w_ready, 1)
                    mm = pe.matmul(ps, lo_w, x_hi[:, 0, k, :], start=False, stop=(k == DK - 1))
                mm.then_inc(up_done, 1)

            pe.wait_ge(zeros_made, 1)
            warm(WARM)
            pe.wait_ge(ident_made, 3)
            turn_x(0)
            turn_x(1)
            warm(WARM_BETWEEN)
            first_up()
            pe.wait_ge(w_ready, 2)
            up(0, 1)
            for u in range(NT):
                unit(fixed(u))
            for m, at in shared_loop(pe):
                unit(at)
            for u in range(U_A, NU):
                unit(fixed(u))
            for n in range(2 * NT - 2, 2 * NT):
                turn_y(n)

        @block.scalar
        def _(act):
            def relu(at, g):
                act.wait_ge(up_done, at.chunk + (g + 1))
                if at.i or g >= RING:
                    act.wait_ge(down_done, at.chunk + (g + 1 - RING))
                act.activation(hid_hi[:, g % RING, :], hid_ps[g % 2][:, :], ACT.Relu).then_inc(hi_done, 1)

            def gelu_chunk(c):
                g = c - NF * U_L1
                act.wait_ge(up_done, c + 1)
                if g == 0:
                    act.wait_ge(bias_loaded, 16 * (1 + 3 * B))
                if g >= 2:
                    act.wait_ge(hid_ready, c - 1)
                act.activation(gelu[:, g % 2, :], hid_ps[g % 2][:, :], ACT.Gelu, bias=b1[:, g % NF:g % NF + 1])\
                    .then_inc(gelu_done, 1)

            def first_set(f):
                act.wait_ge(part_loaded[f // (NF // PARTS)], 48)
                act.copy(w_hi[:, f, :], stage[:, 0, f, :]).then_inc(w_hi_done, 1)

            def x_half(n):
                act.wait_ge(x_turned, n + 1)
                t, k = n // DK, n % DK
                src = out_ps[1][k] if t == 0 else turn_ps
                act.copy(x_hi[:, t, k, :], src[:, :]).then_inc(x_hi_done, 1)

            def split(at, slot, f):
                wset = SPLITS[at.i]
                if wset < M_L1:
                    if f == 0:
                        act.wait_ge(set_loaded, at.set * 6 + 48)
                    act.wait_ge(down_done, at.chunk + (f + 1))
                    act.copy(w_hi[:, f, :], stage[:, slot, f, :]).then_inc(w_hi_done, 1)
                else:
                    act.wait_ge(w_turned, NF * (wset - M_L1) + f + 1)
                    cols = slice(0, WC) if wset == M_L1 else slice(WC - P, WC)
                    act.copy(w_hi[:, f, cols], turn_ps[:, 0:cols.stop - cols.start]).then_inc(w_hi_done, 1)

            def y_copy(n):
                act.wait_ge(y_turned, n + 1)
                t, k = n // DK, n % DK
                act.copy(nat_v[:, t, :, k * P:(k + 1) * P],
                         y_bank(n)[:, :].rearrange("p (j c) -> p j c", c=P)).then_inc(y_rows, 1)

            def exp_of_logits(b):
                act.wait_ge(gate_step, GATE_STEPS * b + 2)
                act.activation(gate_exp[:, b, :], out_ps[0][1][:, 0:4], ACT.Exp, bias=gate_bias[:, b:b + 1])\
                    .then_inc(gate_exp_done, 1)

            def unit(at, slot=None):
                u = at.i
                for f in range(NF):
                    if u == 0 and 1 <= f < HALVES - 1:
                        x_half(f + 1)
                    if u in SPLITS and f:
                        split(at, slot, f - 1)
                    if (u, f - 1) in Y_STEPS:
                        y_copy(Y_STEPS[u, f - 1])
                    if u < U_L1 - 1 or u == U_L1 - 1 and f + 2 < NF:
                        relu(at, f + 2)
                    elif NF * u + f + 2 < NF * NU:
                        gelu_chunk(NF * u + f + 2)
                    if u == 0 and f + 4 < NF:
                        first_set(f + 4)
                    if u in GATE_UNITS and f == 5:
                        exp_of_logits(GATE_UNITS[u])
                    for n in mix_plan.get((u, f), ()):
                        kind, h, k = mix_ops[n]
                        if (kind, k) == ("sum", 4):
                            act.wait_ge(mix_step, mix_sums[n] + 1)
                            act.copy(x_hi[:, h // DK, h % DK, :], share_out[:, 0, h // DK, h % DK, :])\
                                .then_inc(x1_hi_done, 1)
                if u in SPLITS:
                    split(at, slot, NF - 1)

            x_half(0)
            first_set(0)
            x_half(1)
            for f in range(1, 3):
                first_set(f)
            relu(fixed(0), 0)
            first_set(3)
            relu(fixed(0), 1)
            for u in range(NT):
                unit(fixed(u), slot=1)
                if u == 2:
                    act.wait_ge(pair_step, 2 * B)
                    for b in range(B):
                        act.activation(pair_exp[:, b, :], gv[:, b, :], ACT.Exp, scale=10.0,
                                       bias=pair_bias[:, b:b + 1]).then_inc(pair_exp_done, 1)
            for m, at in shared_loop(act):
                unit(at, slot=m - 1)
            for u in range(U_A, NU):
                unit(fixed(u), slot=SPLITS.get(u, 0) % 2)
            for n in range(2 * NT - 2, 2 * NT):
                y_copy(n)

        @block.vector
        def _(dve):
            def relu_lo(at, g):
                dve.wait_ge(hi_done, at.chunk + (g + 1))
                dve.scalar_tensor_tensor(out=hid_lo[:, g % RING, :], in0=hid_ps[g % 2][:, :], scalar=0.0,
                                         in1=hid_hi[:, g % RING, :].bitcast(f32), op0=ALU.max,
                                         op1=ALU.subtract).then_inc(hid_ready, 1)

            def gelu_split(c):
                g = c - NF * U_L1
                dve.wait_ge(gelu_done, g + 1)
                dve.wait_ge(down_done, c + 1 - RING)
                dve.tensor_copy(hid_hi[:, g % RING, :], gelu[:, g % 2, :]).then_inc(gelu_hi, 1)
                dve.wait_ge(gelu_hi, g + 1)
                dve.tensor_tensor(hid_lo[:, g % RING, :], gelu[:, g % 2, :], hid_hi[:, g % RING, :].bitcast(f32),
                                  ALU.subtract).then_inc(hid_ready, 1)

            def first_set(f):
                dve.wait_ge(w_hi_done, f + 1)
                dve.tensor_tensor(w_lo[:, f, :], stage[:, 0, f, :], w_hi[:, f, :].bitcast(f32), ALU.subtract)\
                    .then_inc(w_ready, 1)

            def x_half(n):
                dve.wait_ge(x_hi_done, n + 1)
                t, k = n // DK, n % DK
                src = out_ps[1][k] if t == 0 else turn_ps
                dve.tensor_tensor(x_lo[:, t, k, :], src[:, :], x_hi[:, t, k, :].bitcast(f32), ALU.subtract)\
                    .then_inc(x_ready, 1)

            def split(at, slot, f):
                wset = SPLITS[at.i]
                if wset < M_L1:
                    dve.wait_ge(w_hi_done, at.set + (NF + f + 1))
                    cols, src = slice(0, WC), stage[:, slot, f, :]
                else:
                    dve.wait_ge(w_hi_done, NF * wset + f + 1)
                    cols = slice(0, WC) if wset == M_L1 else slice(WC - P, WC)
                    src = turn_ps[:, 0:cols.stop - cols.start]
                dve.tensor_tensor(w_lo[:, f, cols], src, w_hi[:, f, cols].bitcast(f32), ALU.subtract)\
                    .then_inc(w_ready, 1)

            def take_out(at, m=None):
                u, t = at.i, at.tile
                if u < NU - 1:
                    dve.wait_ge(down_done, at.chunk + NF)
                if u == U_A:
                    dve.wait_ge(pair_step, 5 * B)
                if u == U_L1:
                    dve.wait_ge(bias_loaded, 16 * (1 + 3 * B))
                for k in range(DK):
                    if u == NU - 1:
                        dve.wait_ge(*[(last_half, 1), (down_done, NF * NU)][k])
                    ps = out_ps[u % 2][k][:, :]
                    b = t // TB
                    if u < U_A:
                        dst = share_out[:, m, t, k, :]
                        op = dve.tensor_copy(dst, ps)
                    elif u < U_B:
                        op = dve.tensor_scalar(mix_v[:, t, k, :], ps, pair_w[:, b, 0:1], None, ALU.mult)
                    elif u < U_L1:
                        op = dve.scalar_tensor_tensor(out=mix_v[:, t, k, :], in0=ps, scalar=pair_w[:, b, 1:2],
                                                      in1=mix_v[:, t, k, :], op0=ALU.mult, op1=ALU.add)
                    else:
                        x1 = share_out[:, 0, t, k, :]
                        op = dve.scalar_tensor_tensor(out=x1, in0=ps, scalar=b2[:, b, k:k + 1], in1=x1,
                                                      op0=ALU.add, op1=ALU.add)
                    if u == NU - 1 and k == 0:
                        op.then_inc(last_taken, 1)
                op.then_inc(out_taken, 1)

            def pair_bias_steps():
                dve.wait_ge(gv_loaded, 32 * B)
                for b in range(B):
                    dve.tensor_reduce(pair_max[:, b:b + 1], gv[:, b, 0:4], AX.X, ALU.max).then_inc(pair_step, 1)
                dve.wait_ge(pair_step, B)
                dve.tensor_scalar(pair_bias[:, :], pair_max[:, :], -10.0, None, ALU.mult).then_inc(pair_step, B)

            def pair_weight_steps():
                dve.wait_ge(pair_exp_done, B)
                for b in range(B):
                    dve.tensor_reduce(pair_sum[:, b:b + 1], pair_exp[:, b, 0:4], AX.X, ALU.add)\
                        .then_inc(pair_step, 1)
                dve.wait_ge(pair_step, 3 * B)
                dve.reciprocal(pair_inv[:, :], pair_sum[:, :]).then_inc(pair_step, B)
                dve.wait_ge(pair_step, 4 * B)
                for b in range(B):
                    dve.tensor_scalar(pair_w[:, b, :], pair_exp[:, b, 4:6], pair_inv[:, b:b + 1], None, ALU.mult)\
                        .then_inc(pair_step, 1)

            def gate_term(b, n):
                count = GATE_TERMS * b + gate_order.index(n)
                t, k = TB * b, n % DK
                col = mix_v[:, t, k, 0:1] if n < DK else share_out[:, n // DK - 1, t, k, 0:1]
                if count == 0:
                    dve.wait_ge(gw_loaded, 32)
                if n == gate_order[0]:
                    if b:
                        dve.wait_ge(gate_up, b)
                    op = dve.tensor_scalar(gate_part[:, :], gw1[:, n, :], col, None, ALU.mult)
                else:
                    dve.wait_ge(gate_sums, count)
                    if n == 0:
                        dve.wait_ge(out_taken, U_B + TB * b + 1)
                    op = dve.scalar_tensor_tensor(out=gate_part[:, :], in0=gw1[:, n, :], scalar=col,
                                                  in1=gate_part[:, :], op0=ALU.mult, op1=ALU.add)
                op.then_inc(gate_sums, 1)

            def gate_hidden(b):
                dve.wait_ge(gate_up, b + 1)
                for half in range(DK):
                    op = dve.tensor_scalar(gate_hid[:, half, :], zeros[:, :], out_ps[0][0][:, half:half + 1], 0.0,
                                           ALU.add, ALU.max)
                op.then_inc(gate_hid_done, 1)

            def gate_maximum(b):
                dve.wait_ge(gate_logits, b + 1)
                dve.tensor_reduce(gate_max[:, b:b + 1], out_ps[0][1][:, 0:4], AX.X, ALU.max).then_inc(gate_step, 1)
                dve.wait_ge(gate_step, GATE_STEPS * b + 1)
                dve.tensor_scalar(gate_bias[:, b:b + 1], gate_max[:, b:b + 1], -1.0, None, ALU.mult)\
                    .then_inc(gate_step, 1)

            def gate_softmax(b):
                dve.wait_ge(gate_exp_done, b + 1)
                dve.tensor_reduce(gate_sum[:, b:b + 1], gate_exp[:, b, :], AX.X, ALU.add).then_inc(gate_step, 1)
                dve.wait_ge(gate_step, GATE_STEPS * b + 3)
                dve.reciprocal(gate_inv[:, b:b + 1], gate_sum[:, b:b + 1]).then_inc(gate_step, 1)
                dve.wait_ge(gate_step, GATE_STEPS * b + 4)
                dve.tensor_scalar(gate[:, b, :], gate_exp[:, b, :], gate_inv[:, b:b + 1], None, ALU.mult)\
                    .then_inc(gate_step, 1)

            def mixture(n):
                kind, h, k = mix_ops[n]
                t, half = h // DK, h % DK
                x1 = share_out[:, 0, t, half, :]
                hi, lo = x_hi[:, t, half, :], x_lo[:, t, half, :]
                if kind == "lo":
                    dve.wait_ge(x1_hi_done, h + 1)
                    dve.tensor_tensor(lo, x1, hi.bitcast(f32), ALU.subtract).then_inc(x1_split, 1)
                    return
                g = gate[:, t // TB, :]
                if k == 0:
                    dve.wait_ge(gate_step, GATE_STEPS * (t // TB + 1))
                else:
                    dve.wait_ge(mix_step, mix_sums[n])
                if k == 4:
                    op = dve.tensor_tensor(x1, x1, lo.bitcast(f32), ALU.add)
                else:
                    a, w, c = [(x1, 1, hi.bitcast(f32)), (mix_v[:, t, half, :], 0, x1),
                               (share_out[:, 1, t, half, :], 2, x1), (share_out[:, 2, t, half, :], 3, x1)][k]
                    op = dve.scalar_tensor_tensor(out=x1, in0=a, scalar=g[:, w:w + 1], in1=c, op0=ALU.mult,
                                                  op1=ALU.add)
                op.then_inc(mix_step, 1)

            def unit(at, slot=None, m=None):
                u = at.i
                for f in range(NF):
                    if u == 0 and 1 <= f < HALVES - 1:
                        x_half(f + 1)
                    for n in mix_plan.get((u, f), ()):
                        mixture(n)
                    if u in SPLITS and f:
                        split(at, slot, f - 1)
                    if (u, f) in gate_plan:
                        gate_term(*gate_plan[u, f])
                    if u in GATE_UNITS and f == 3:
                        gate_hidden(GATE_UNITS[u])
                    if u in GATE_UNITS and f == 5:
                        gate_maximum(GATE_UNITS[u])
                    if u in GATE_UNITS and f == 6:
                        gate_softmax(GATE_UNITS[u])
                    if u < U_L1 - 1 or u == U_L1 - 1 and f + 2 < NF:
                        relu_lo(at, f + 2)
                    elif NF * u + f + 2 < NF * NU:
                        gelu_split(NF * u + f + 2)
                    if u == 0 and f + 4 < NF:
                        first_set(f + 4)
                take_out(at, m)
                if u in SPLITS:
                    split(at, slot, NF - 1)

            x_half(0)
            first_set(0)
            x_half(1)
            for f in range(1, 3):
                first_set(f)
            relu_lo(fixed(0), 0)
            first_set(3)
            relu_lo(fixed(0), 1)
            for u in range(NT):
                unit(fixed(u), slot=1, m=0)
                if u == 1:
                    pair_bias_steps()
                if u == 3:
                    pair_weight_steps()
            for m, at in shared_loop(dve):
                unit(at, slot=m - 1, m=m)
            for u in range(U_A, NU):
                unit(fixed(u), slot=SPLITS.get(u, 0) % 2)


_INS = ['x', 'itok_B_0_2', 'itok_B_0_15', 'L0_cond_expert_wi', 'L0_cond_expert_wo', 'L0_cond_share_wi',
        'L0_cond_share_wo', 'L0_cond_gate_vecs', 'L0_cond_gate_w1', 'L0_cond_gate_w2', 'L1_cond_fc1_w',
        'L1_cond_fc1_b', 'L1_cond_fc2_w', 'L1_cond_fc2_b', 'L1_cond_experts_w', 'L1_cond_experts_b']


def kernel(**inputs):
    import numpy as _np
    import concourse.bacc as _bacc
    from concourse import mybir as _mybir
    from concourse.bass_utils import run_bass_kernel_spmd as _run

    nc = _bacc.Bacc("TRN2", target_bir_lowering=False, num_devices=1)
    arrays, args = {}, []
    for name in _INS:
        a = _np.ascontiguousarray(inputs[name])
        arrays[f"in_{name}_dram"] = a
        args.append(nc.dram_tensor(f"in_{name}_dram", a.shape, _mybir.dt.from_np(a.dtype), kind="ExternalInput").ap())
    x = inputs['x']
    args.append(nc.dram_tensor("out_0_dram", x.shape, _mybir.dt.float32, kind="ExternalOutput").ap())
    residual_moe_program(nc, *args)
    r = _run(nc, [arrays], core_ids=[0])
    return r.results[0]["out_0_dram"]
```

```python
import concourse.bass as bass
from concourse import mybir
from contextlib import ExitStack


def residual_moe_program(nc, x, itok_gate, itok_part, expert_wi, expert_wo, share_wi, share_wo, gate_vecs,
                         gate_w1, gate_w2, fc1_w, fc1_b, fc2_w, fc2_b, experts_w, experts_b, out):
    f32 = mybir.dt.float32
    f32r = mybir.dt.float32r
    i32 = mybir.dt.int32
    ALU = mybir.AluOpType
    ACT = mybir.ActivationFunctionType
    AX = mybir.AxisListType

    P = 128
    B, S, D = x.shape
    F = share_wi.shape[2]
    SHARED = fc2_w.shape[0]
    NSH = share_wi.shape[0]
    NE = expert_wi.shape[0]
    NPART = experts_w.shape[0]
    T = 512
    NT = B * S // T
    TB = S // T
    DK = D // P
    NF = F // P
    WC = DK * P + D
    RING = 4
    PARTS = 4
    SHARPNESS = 10.0
    REST = SHARED - P

    U_A = NSH * NT
    U_B = U_A + NT
    U_L1 = U_B + NT
    NU = U_L1 + NT

    def first_unit(m):
        return m * NT if m <= NSH else U_A + (m - NSH) * TB

    M_A, M_B, M_L1 = NSH, NSH + B, NSH + 2 * B

    Q = 32
    NQ = P // Q

    x_nat_dram = x.rearrange("b (n p) d -> p (b n) d", p=P)
    out_dram = out.rearrange("b (n p) d -> p (b n) d", p=P)

    ctx = ExitStack()
    with ctx:
        def sb(name, shape, dt=f32):
            return ctx.enter_context(nc.sbuf_tensor(name, shape, dt))

        def sem(name):
            return ctx.enter_context(nc.semaphore(name))

        w_hi = sb("w_hi", [P, NF, WC], f32r)
        w_lo = sb("w_lo", [P, NF, WC], f32r)
        stage = sb("stage", [P, 2, NF, WC])
        x_hi = sb("x_hi", [P, NT, DK, T], f32r)
        x_lo = sb("x_lo", [P, NT, DK, T], f32r)
        hid_hi = sb("hid_hi", [P, RING, T], f32r)
        hid_lo = sb("hid_lo", [P, RING, T], f32r)
        gelu = sb("gelu", [P, 2, T])
        share_out = sb("share_out", [P, NSH, NT, DK, T])
        mix = sb("mix", [P, NT, DK * T])
        gw1 = sb("gw1", [P, (1 + NSH) * DK, D])
        gw2 = sb("gw2", [P, DK, 4])
        ident = sb("ident", [P, P])
        zeros = sb("zeros", [P, P])
        ones = sb("ones", [P, 1])
        gate_part = sb("gate_part", [P, D])
        gate_hid = sb("gate_hid", [P, DK, P])
        idx = sb("idx", [1, 2 * B], i32)
        b1 = sb("b1", [P, NF])
        b2 = sb("b2", [P, B, DK])
        gv = sb("gv", [P, B, 6])
        pair_max = sb("pair_max", [P, B])
        pair_bias = sb("pair_bias", [P, B])
        pair_exp = sb("pair_exp", [P, B, 6])
        pair_sum = sb("pair_sum", [P, B])
        pair_inv = sb("pair_inv", [P, B])
        pair_w = sb("pair_w", [P, B, 2])
        gate_max = sb("gate_max", [P, B])
        gate_bias = sb("gate_bias", [P, B])
        gate_exp = sb("gate_exp", [P, B, 4])
        gate_sum = sb("gate_sum", [P, B])
        gate_inv = sb("gate_inv", [P, B])
        gate = sb("gate", [P, B, 4])

        l1_stage = stage[:, M_L1 % 2, :, :].rearrange("p f w -> p (f w)")
        FQ = F // NQ
        fc1_v = l1_stage[:, 0:DK * F].rearrange("p (k h) -> p k h", k=DK)
        fc2_v = l1_stage[:, DK * F:].rearrange("p (j h) -> p j h", h=FQ)
        rows_raw, rows_turned = l1_stage[:, 0:T], l1_stage[:, T:2 * T]
        rows_v = rows_turned.rearrange("p (j h) -> p j h", h=FQ)
        DJ, SJ = D // Q, SHARED // Q

        mix_v = mix[:, :, :].rearrange("p t (k n) -> p t k n", k=DK)
        nat_v = mix[:, :, :].rearrange("p t (j d) -> p t j d", d=D)

        def bank(name):
            return ctx.enter_context(nc.psum_tensor(name, [P, T], f32))

        hid_ps = [bank(f"hid_ps{i}") for i in range(2)]
        out_ps = [[bank(f"out_ps{i}{k}") for k in range(DK)] for i in range(2)]
        turn_ps = bank("turn_ps")

        x_loaded = [sem(f"x_loaded{t}") for t in range(NT)]
        x_first = sem("x_first")
        part_loaded = [sem(f"part_loaded{i}") for i in range(PARTS)]
        set_loaded = sem("set_loaded")
        l1_loaded = sem("l1_loaded")
        rows_loaded = sem("rows_loaded")
        idx_loaded = sem("idx_loaded")
        gv_loaded = sem("gv_loaded")
        gw_loaded = sem("gw_loaded")
        bias_loaded = sem("bias_loaded")
        out_stored = sem("out_stored")
        zeros_made = sem("zeros_made")
        ident_made = sem("ident_made")
        x_turned = sem("x_turned")
        x_bounced = sem("x_bounced")
        x_hi_done = sem("x_hi_done")
        x_ready = sem("x_ready")
        up_done = sem("up_done")
        hi_done = sem("hi_done")
        gelu_done = sem("gelu_done")
        gelu_hi = sem("gelu_hi")
        hid_ready = sem("hid_ready")
        down_done = sem("down_done")
        w_turned = sem("w_turned")
        w_placed = sem("w_placed")
        rows_done = sem("rows_done")
        w_hi_done = sem("w_hi_done")
        w_ready = sem("w_ready")
        out_taken = sem("out_taken")
        pair_step = sem("pair_step")
        pair_exp_done = sem("pair_exp_done")
        gate_sums = sem("gate_sums")
        gate_up = sem("gate_up")
        last_half = sem("last_half")
        last_taken = sem("last_taken")
        gate_hid_done = sem("gate_hid_done")
        gate_logits = sem("gate_logits")
        gate_step = sem("gate_step")
        gate_exp_done = sem("gate_exp_done")
        mix_step = sem("mix_step")
        x1_hi_done = sem("x1_hi_done")
        x1_split = sem("x1_split")
        y_turned = sem("y_turned")
        y_rows = sem("y_rows")

        block = ctx.enter_context(nc.Block())

        def set_of(u):
            return u // NT if u < U_A else (M_A + (u - U_A) // TB if u < U_L1 else M_L1)

        SPLITS = {first_unit(m) - 1: m for m in range(1, M_L1 + 1)}
        ROWS_UNIT = U_L1 + TB - 1
        SPLITS[ROWS_UNIT] = M_L1 + 1
        TURN_UNIT = U_B + 2
        X_STEPS = {(0, 3): 2, (0, 4): 3, (1, 1): 4, (1, 2): 5, (2, 1): 6, (2, 2): 7}
        GATE_UNITS = {U_B + TB * b + 1: b for b in range(B)}
        Y_STEPS = {(U_L1 + 2, 1 + n): n for n in range(4)}
        Y_STEPS.update({(U_L1 + 3, 1): 4, (U_L1 + 3, 2): 5})

        HALVES = NT * DK
        mix_ops = []
        for h in range(HALVES):
            mix_ops += [("sum", h, k) for k in range(2)]
            if h:
                mix_ops.append(("lo", h - 1, 0))
            mix_ops += [("sum", h, k) for k in range(2, 5)]
        mix_ops.append(("lo", HALVES - 1, 0))
        mix_at = {op: n for n, op in enumerate(mix_ops)}
        MIX_RATE = {U_B + 2: 1, U_B + 3: 1, U_L1: 2, U_L1 + 1: 1, U_L1 + 2: 2}
        mix_plan, planned = {}, 0
        for u, rate in MIX_RATE.items():
            for f in range(NF):
                mix_plan[u, f] = range(planned, min(planned + rate, len(mix_ops)))
                planned = mix_plan[u, f].stop
        assert planned == len(mix_ops)

        GATE_TERMS = (1 + NSH) * DK
        gate_plan = {}
        for u, b in GATE_UNITS.items():
            for n in range(DK, GATE_TERMS):
                gate_plan[u - 1, n - DK] = (b, n)
            for n in range(DK):
                gate_plan[u, n] = (b, n)
        gate_order = list(range(DK, GATE_TERMS)) + list(range(DK))
        WARM = 6
        WARM_BETWEEN = 2
        GATE_STEPS = 5
        mix_sums = [sum(kind == "sum" for kind, _, _ in mix_ops[:n]) for n in range(len(mix_ops))]

        def y_bank(n):
            return hid_ps[0] if n == 2 * NT - 1 else turn_ps

        def weight_parts(wset, slot, f, dst):
            if wset < M_L1:
                return [(dst[:, f, :], stage[:, slot, f, :])]
            if wset == M_L1:
                up = fc1_v.rearrange("p k (q g) -> p k q g", q=NQ)[:, :, :, f * Q:(f + 1) * Q]
                return [(dst[:, f, 0:DK * P].rearrange("p (k q c) -> p k q c", k=DK, q=NQ), up),
                        (dst[:, f, DK * P:WC].rearrange("p (j c) -> p j c", c=Q), fc2_v[:, :, f * Q:(f + 1) * Q])]
            return [(dst[:, f, DK * P + SHARED:WC].rearrange("p (j c) -> p j c", c=Q),
                     rows_v[:, :, f * Q:(f + 1) * Q])]

        class Place:

            def __init__(self, i, unit, chunk, wset):
                self.i, self.tile, self.unit, self.chunk, self.set = i, i % NT, unit, chunk, wset

        def fixed(u):
            return Place(u, u, NF * u, NF * set_of(u))

        def shared_loop(eng):
            with eng.Fori(1, NSH) as m:
                units = eng.snap(m * NT)
                chunks = eng.snap(m * (NT * NF))
                sets = eng.snap(m * NF)
                for t in range(NT):
                    yield m, Place(NT + t, units + t, chunks + NF * t, sets)

        @block.sync
        def _(sp):
            def load_set(i, wi, wo, fs, loaded):
                cols = slice(fs.start * P, fs.stop * P)
                for k in range(DK):
                    sp.dma_start(stage[:, i, fs, k * P:(k + 1) * P],
                                 wi[k * P:(k + 1) * P, cols].rearrange("p (f c) -> p f c", c=P))\
                        .then_inc(loaded, 16)
                sp.dma_start(stage[:, i, fs, DK * P:WC], wo[cols, :].rearrange("(f p) d -> p f d", p=P))\
                    .then_inc(loaded, 16)

            sp.dma_start(nat_v[:, 0, 0:2, :], x_nat_dram[:, 0:2, :]).then_inc(x_first, 16)
            sp.dma_start(nat_v[:, 0, 2:4, :], x_nat_dram[:, 2:4, :]).then_inc(x_loaded[0], 16)
            step = NF // PARTS
            for n in range(PARTS):
                load_set(0, share_wi[0], share_wo[0], slice(n * step, (n + 1) * step), part_loaded[n])
            def load_x(t):
                src = x.rearrange("b s d -> (b s) d")[t * T:(t + 1) * T, :]\
                    .rearrange("(j i) (k q c) -> i j k q c", i=Q, k=DK, q=NQ)
                for k in range(DK):
                    for q in range(NQ):
                        dst = mix_v[q * Q:(q + 1) * Q, t, k, :].rearrange("i (j c) -> i j c", c=Q)
                        sp.dma_start(dst, src[:, :, k, q, :]).then_inc(x_loaded[t], 16)

            whole = slice(0, NF)
            load_x(1)
            load_set(1, share_wi[1], share_wo[1], whole, set_loaded)
            for t in range(2, NT):
                load_x(t)

            sp.dma_start(idx[0:1, 0:B], itok_gate.rearrange("(a n) -> a n", a=1)).then_inc(idx_loaded, 16)
            sp.dma_start(idx[0:1, B:2 * B], itok_part.rearrange("(a n) -> a n", a=1)).then_inc(idx_loaded, 16)
            sp.dma_start(gw1[:, :, :], gate_w1.rearrange("(n p) d -> p n d", p=P)).then_inc(gw_loaded, 16)
            sp.dma_start(gw2[:, :, :], gate_w2.rearrange("(n p) d -> p n d", p=P)).then_inc(gw_loaded, 16)
            sp.wait_ge(idx_loaded, 32)
            t_idx = [sp.value_load(idx[0:1, b:b + 1], min_val=0, max_val=NE - 2) for b in range(B)]
            e_idx = [sp.value_load(idx[0:1, B + b:B + b + 1], min_val=0, max_val=NPART - 1) for b in range(B)]
            gv_flat = gate_vecs.rearrange("a c -> (a c)")
            col = lambda v: v.rearrange("(p a) -> p a", a=1)
            with nc.allow_non_contiguous_dma(reason="biases, one element a partition"):
                for q in range(NQ):
                    sp.dma_start(b1[q * Q:(q + 1) * Q, :], fc1_b[q * FQ:(q + 1) * FQ]
                                 .rearrange("(f i) -> i f", i=Q)).then_inc(bias_loaded, 16)
                for b in range(B):
                    row = gate_vecs[bass.ds(t_idx[b], 1), :].rearrange("a c -> (a c)")
                    sp.dma_start(gv[:, b, 0:4], row.partition_broadcast(P)).then_inc(gv_loaded, 16)
                    sp.dma_start(gv[:, b, 4:6], gv_flat[bass.ds(t_idx[b] * (NE + 1), 2)].partition_broadcast(P))\
                        .then_inc(gv_loaded, 16)
                    sp.dma_start(b2[:, b, 0:1], col(fc2_b[0:P])).then_inc(bias_loaded, 16)
                    sp.dma_start(b2[0:REST, b, 1:2], col(fc2_b[P:SHARED])).then_inc(bias_loaded, 16)
                    sp.dma_start(b2[REST:P, b, 1:2], experts_b[bass.ds(e_idx[b], 1), :].rearrange("a p -> p a"))\
                        .then_inc(bias_loaded, 16)

            for m in range(2, M_L1):
                sp.wait_ge(w_ready, NF * (m - 1))
                sp.wait_ge(set_loaded, 48 * (m - 1))
                if m < M_A:
                    load_set(m % 2, share_wi[m], share_wo[m], whole, set_loaded)
                else:
                    e, b = (m - M_A) // B, (m - M_A) % B
                    at = bass.ds(t_idx[b] + e, 1)
                    load_set(m % 2, expert_wi[at, :, :].rearrange("a d f -> (a d) f"),
                             expert_wo[at, :, :].rearrange("a f d -> (a f) d"), whole, set_loaded)

            def load_rows(dst, b, loaded):
                for q in range(NQ):
                    src = experts_w[bass.ds(e_idx[b], 1), :, :].rearrange("a (j i) h -> i (a j) h", i=Q)
                    sp.dma_start(dst[q * Q:(q + 1) * Q], src[:, :, q * FQ:(q + 1) * FQ]).then_inc(loaded, 16)

            sp.wait_ge(w_ready, NF * (M_L1 - 1))
            for q in range(NQ):
                part = slice(q * Q, (q + 1) * Q)
                for k in range(DK):
                    cols = slice(k * P + q * Q, k * P + (q + 1) * Q)
                    sp.dma_start(fc1_v[part, k, :].rearrange("i (j c) -> i j c", c=Q),
                                 fc1_w[:, cols].rearrange("(j i) c -> i j c", i=Q)).then_inc(l1_loaded, 16)
                sp.dma_start(fc2_v[part, 0:SJ, :], fc2_w[:, q * FQ:(q + 1) * FQ].rearrange("(j i) h -> i j h", i=Q))\
                    .then_inc(l1_loaded, 16)
            load_rows(fc2_v[:, SJ:DJ, :], 0, l1_loaded)
            sp.wait_ge(w_ready, NF * (M_L1 + 1))
            load_rows(rows_raw.rearrange("p (j h) -> p j h", h=FQ), 1, rows_loaded)

            for n in range(2 * NT):
                t, cols = n // DK, slice(n % DK * P, (n % DK + 1) * P)
                sp.wait_ge(y_rows, n + 1)
                sp.dma_start(out_dram[:, 4 * t:4 * t + 4, cols], nat_v[:, t, :, cols]).then_inc(out_stored, 16)
            sp.wait_ge(out_stored, 16 * 2 * NT)

        @block.gpsimd
        def _(pool):
            pool.memset(zeros[:, :], 0.0).then_inc(zeros_made, 1)
            pool.memset(ones[:, :], 1.0).then_inc(ident_made, 1)
            pool.memset(ident[:, :], 0.0).then_inc(ident_made, 1)
            pool.wait_ge(ident_made, 2)
            pool.affine_select(out=ident[:, :], in_=ident[:, :], compare_op=ALU.not_equal, fill=1.0, base=0,
                               pattern=[[-1, P]], channel_multiplier=1).then_inc(ident_made, 1)

        @block.tensor
        def _(pe):
            def product(ps, hi_w, lo_w, hi_m, lo_m, start, stop):
                pe.matmul(ps, hi_w, hi_m, start=start, stop=False)
                pe.matmul(ps, hi_w, lo_m, start=False, stop=False)
                return pe.matmul(ps, lo_w, hi_m, start=False, stop=stop)

            def up(tile, f):
                for k in range(DK):
                    cols = slice(k * P, (k + 1) * P)
                    mm = product(hid_ps[f % 2][:, :], w_hi[:, f, cols], w_lo[:, f, cols],
                                 x_hi[:, tile, k, :], x_lo[:, tile, k, :], k == 0, k == DK - 1)
                mm.then_inc(up_done, 1)

            def down(parity, f, last=False):
                for k in range(DK):
                    cols = slice((DK + k) * P, (DK + k + 1) * P)
                    mm = product(out_ps[parity][k][:, :], w_hi[:, f, cols], w_lo[:, f, cols],
                                 hid_hi[:, f % RING, :], hid_lo[:, f % RING, :], f == 0, f == NF - 1)
                    if last and k == 0:
                        mm.then_inc(last_half, 1)
                mm.then_inc(down_done, 1)

            def turn_x(n):
                for j in range(T // P):
                    if n == 0 and j % 2 == 0:
                        pe.wait_ge([x_first, x_loaded[0]][j // 2], 16)
                    mm = pe.transpose(out_ps[1][n][:, j * P:(j + 1) * P], nat_v[:, 0, j, n * P:(n + 1) * P],
                                      ident[:, :])
                mm.then_inc(x_turned, 1)

            def turn_y(n):
                t, k = n // DK, n % DK
                if n == 2 * NT - 2:
                    pe.wait_ge(last_taken, 1)
                else:
                    pe.wait_ge(out_taken, U_L1 + t + 1)
                if 0 < n < 2 * NT - 1:
                    pe.wait_ge(y_rows, n)
                for j in range(T // P):
                    cols = slice(j * P, (j + 1) * P)
                    mm = pe.transpose(y_bank(n)[:, cols], share_out[:, 0, t, k, cols], ident[:, :])
                mm.then_inc(y_turned, 1)

            def gate_first(b):
                pe.wait_ge(out_taken, U_B + TB * b + 1)
                pe.wait_ge(gate_sums, GATE_TERMS * (b + 1))
                for half in range(DK):
                    mm = pe.matmul(out_ps[0][0][:, half:half + 1], gate_part[:, half * P:(half + 1) * P],
                                   ones[:, :], start=True, stop=True)
                mm.then_inc(gate_up, 1)

            def gate_second(b):
                if b == 0:
                    pe.wait_ge(gw_loaded, 32)
                pe.wait_ge(gate_hid_done, b + 1)
                for half in range(DK):
                    mm = pe.matmul(out_ps[0][1][:, 0:4], gate_hid[:, half, :], gw2[:, half, :],
                                   start=(half == 0), stop=(half == DK - 1))
                mm.then_inc(gate_logits, 1)

            def unit(at):
                u = at.i
                for f in range(NF):
                    pe.wait_ge(hid_ready, at.chunk + (f + 1))
                    if f + 2 < NF:
                        if u == first_unit(set_of(u)):
                            pe.wait_ge(w_ready, at.set + (f + 3))
                        up(at.tile, f + 2)
                    elif u + 1 < NU:
                        if u + 1 == first_unit(set_of(u + 1)):
                            pe.wait_ge(w_ready, at.set + (f + 3))
                        if f + 2 == NF and u + 1 < NT:
                            pe.wait_ge(x_ready, DK * (u + 2))
                        if f + 2 == NF and u + 1 >= U_L1:
                            pe.wait_ge(x1_split, DK * (u + 2 - U_L1))
                        up((at.tile + 1) % NT, f + 2 - NF)
                    if f == 0 and u >= 2:
                        pe.wait_ge(out_taken, at.unit + (-1))
                    if f == 0 and u in (U_B + 2, U_L1):
                        pe.wait_ge(gate_exp_done, (u - U_B) // 2)
                    if u == ROWS_UNIT + 1:
                        pe.wait_ge(w_ready, NF * (M_L1 + 1) + f + 1)
                    down(u % 2, f, last=(u == NU - 1 and f == NF - 1))
                    if u in GATE_UNITS and f == 2:
                        gate_first(GATE_UNITS[u])
                    if u in GATE_UNITS and f == 4:
                        gate_second(GATE_UNITS[u])
                    if (u, f) in Y_STEPS:
                        turn_y(Y_STEPS[u, f])

            def warm(n):
                for _ in range(n):
                    pe.matmul(out_ps[0][0][:, 0:P], zeros[:, :], zeros[:, :], start=True, stop=True)

            def first_up():
                ps = hid_ps[0][:, :]
                for k in range(DK):
                    hi_w, lo_w = (w[:, 0, k * P:(k + 1) * P] for w in (w_hi, w_lo))
                    pe.wait_ge(x_hi_done, k + 1)
                    if k == 0:
                        pe.wait_ge(w_hi_done, 1)
                    pe.matmul(ps, hi_w, x_hi[:, 0, k, :], start=(k == 0), stop=False)
                    pe.wait_ge(x_ready, k + 1)
                    pe.matmul(ps, hi_w, x_lo[:, 0, k, :], start=False, stop=False)
                    if k == 0:
                        pe.wait_ge(w_ready, 1)
                    mm = pe.matmul(ps, lo_w, x_hi[:, 0, k, :], start=False, stop=(k == DK - 1))
                mm.then_inc(up_done, 1)

            pe.wait_ge(zeros_made, 1)
            warm(WARM)
            pe.wait_ge(ident_made, 3)
            turn_x(0)
            turn_x(1)
            warm(WARM_BETWEEN)
            first_up()
            pe.wait_ge(w_ready, 2)
            up(0, 1)
            for u in range(NT):
                unit(fixed(u))
            for m, at in shared_loop(pe):
                unit(at)
            for u in range(U_A, NU):
                unit(fixed(u))
            for n in range(2 * NT - 2, 2 * NT):
                turn_y(n)

        @block.scalar
        def _(act):
            def relu(at, g):
                act.wait_ge(up_done, at.chunk + (g + 1))
                if at.i or g >= RING:
                    act.wait_ge(down_done, at.chunk + (g + 1 - RING))
                act.activation(hid_hi[:, g % RING, :], hid_ps[g % 2][:, :], ACT.Relu).then_inc(hi_done, 1)

            def gelu_chunk(c):
                g = c - NF * U_L1
                act.wait_ge(up_done, c + 1)
                if g == 0:
                    act.wait_ge(bias_loaded, 16 * (NQ + 3 * B))
                if g >= 2:
                    act.wait_ge(hid_ready, c - 1)
                act.activation(gelu[:, g % 2, :], hid_ps[g % 2][:, :], ACT.Gelu, bias=b1[:, g % NF:g % NF + 1])\
                    .then_inc(gelu_done, 1)

            def first_set(f):
                act.wait_ge(part_loaded[f // (NF // PARTS)], 48)
                act.copy(w_hi[:, f, :], stage[:, 0, f, :]).then_inc(w_hi_done, 1)

            def x_half(n):
                t, k = n // DK, n % DK
                if t == 0:
                    act.wait_ge(x_turned, n + 1)
                    src = out_ps[1][k][:, :]
                else:
                    act.wait_ge(x_bounced, n - DK + 1)
                    src = gelu[:, k, :]
                act.copy(x_hi[:, t, k, :], src).then_inc(x_hi_done, 1)

            def place(f):
                act.wait_ge(w_turned, f + 1)
                act.copy(l1_stage[:, f * T:(f + 1) * T], gelu[:, f % 2, :]).then_inc(w_placed, 1)

            def split(at, slot, f):
                wset = SPLITS[at.i]
                if wset < M_L1 and f == 0:
                    act.wait_ge(set_loaded, at.set * 6 + 48)
                act.wait_ge(down_done, at.chunk + (f + 1))
                if wset == M_L1 and f == 0:
                    act.wait_ge(w_placed, NF)
                if wset == M_L1 + 1 and f == 0:
                    act.wait_ge(rows_done, 1)
                for dst, src in weight_parts(wset, slot, f, w_hi):
                    op = act.copy(dst, src)
                op.then_inc(w_hi_done, 1)

            def y_copy(n):
                act.wait_ge(y_turned, n + 1)
                t, k = n // DK, n % DK
                act.copy(nat_v[:, t, :, k * P:(k + 1) * P],
                         y_bank(n)[:, :].rearrange("p (j c) -> p j c", c=P)).then_inc(y_rows, 1)

            def exp_of_logits(b):
                act.wait_ge(gate_step, GATE_STEPS * b + 2)
                act.activation(gate_exp[:, b, :], out_ps[0][1][:, 0:4], ACT.Exp, bias=gate_bias[:, b:b + 1])\
                    .then_inc(gate_exp_done, 1)

            def unit(at, slot=None):
                u = at.i
                for f in range(NF):
                    if (u, f) in X_STEPS:
                        x_half(X_STEPS[u, f])
                    if u == TURN_UNIT:
                        place(f)
                    if u in SPLITS and f:
                        split(at, slot, f - 1)
                    if (u, f - 1) in Y_STEPS:
                        y_copy(Y_STEPS[u, f - 1])
                    if u < U_L1 - 1 or u == U_L1 - 1 and f + 2 < NF:
                        relu(at, f + 2)
                    elif NF * u + f + 2 < NF * NU:
                        gelu_chunk(NF * u + f + 2)
                    if u == 0 and f + 4 < NF:
                        first_set(f + 4)
                    if u in GATE_UNITS and f == 5:
                        exp_of_logits(GATE_UNITS[u])
                    for n in mix_plan.get((u, f), ()):
                        kind, h, k = mix_ops[n]
                        if (kind, k) == ("sum", 4):
                            act.wait_ge(mix_step, mix_sums[n] + 1)
                            act.copy(x_hi[:, h // DK, h % DK, :], share_out[:, 0, h // DK, h % DK, :])\
                                .then_inc(x1_hi_done, 1)
                if u in SPLITS:
                    split(at, slot, NF - 1)

            x_half(0)
            first_set(0)
            x_half(1)
            for f in range(1, 3):
                first_set(f)
            relu(fixed(0), 0)
            first_set(3)
            relu(fixed(0), 1)
            for u in range(NT):
                unit(fixed(u), slot=1)
                if u == 2:
                    act.wait_ge(pair_step, 2 * B)
                    for b in range(B):
                        act.activation(pair_exp[:, b, :], gv[:, b, :], ACT.Exp, scale=SHARPNESS,
                                       bias=pair_bias[:, b:b + 1]).then_inc(pair_exp_done, 1)
            for m, at in shared_loop(act):
                unit(at, slot=m - 1)
            for u in range(U_A, NU):
                unit(fixed(u), slot=SPLITS.get(u, 0) % 2)
            for n in range(2 * NT - 2, 2 * NT):
                y_copy(n)

        @block.vector
        def _(dve):
            def relu_lo(at, g):
                dve.wait_ge(hi_done, at.chunk + (g + 1))
                dve.scalar_tensor_tensor(out=hid_lo[:, g % RING, :], in0=hid_ps[g % 2][:, :], scalar=0.0,
                                         in1=hid_hi[:, g % RING, :].bitcast(f32), op0=ALU.max,
                                         op1=ALU.subtract).then_inc(hid_ready, 1)

            def gelu_split(c):
                g = c - NF * U_L1
                dve.wait_ge(gelu_done, g + 1)
                dve.wait_ge(down_done, c + 1 - RING)
                dve.tensor_copy(hid_hi[:, g % RING, :], gelu[:, g % 2, :]).then_inc(gelu_hi, 1)
                dve.wait_ge(gelu_hi, g + 1)
                dve.tensor_tensor(hid_lo[:, g % RING, :], gelu[:, g % 2, :], hid_hi[:, g % RING, :].bitcast(f32),
                                  ALU.subtract).then_inc(hid_ready, 1)

            def first_set(f):
                dve.wait_ge(w_hi_done, f + 1)
                dve.tensor_tensor(w_lo[:, f, :], stage[:, 0, f, :], w_hi[:, f, :].bitcast(f32), ALU.subtract)\
                    .then_inc(w_ready, 1)

            def x_half(n):
                dve.wait_ge(x_hi_done, n + 1)
                t, k = n // DK, n % DK
                src = out_ps[1][k][:, :] if t == 0 else gelu[:, k, :]
                dve.tensor_tensor(x_lo[:, t, k, :], src, x_hi[:, t, k, :].bitcast(f32), ALU.subtract)\
                    .then_inc(x_ready, 1)

            def x_turn(n):
                t, k = n // DK, n % DK
                if k == 0:
                    dve.wait_ge(x_loaded[t], 16 * DK * NQ)
                if n >= 2 * DK:
                    dve.wait_ge(x_ready, n - 1)
                dve.transpose(gelu[:, k, :], mix_v[:, t, k, :]).then_inc(x_bounced, 1)

            def turn_piece(f):
                if f == 0:
                    dve.wait_ge(l1_loaded, 16 * NQ * (DK + 2))
                if f >= 2:
                    dve.wait_ge(w_placed, f - 1)
                dve.transpose(gelu[:, f % 2, :], l1_stage[:, f * T:(f + 1) * T]).then_inc(w_turned, 1)

            def split(at, slot, f):
                wset = SPLITS[at.i]
                if wset < M_L1:
                    dve.wait_ge(w_hi_done, at.set + (NF + f + 1))
                else:
                    dve.wait_ge(w_hi_done, NF * wset + f + 1)
                for (dst, src), (hi, _) in zip(weight_parts(wset, slot, f, w_lo), weight_parts(wset, slot, f, w_hi)):
                    op = dve.tensor_tensor(dst, src, hi.bitcast(f32), ALU.subtract)
                op.then_inc(w_ready, 1)

            def take_out(at, m=None):
                u, t = at.i, at.tile
                if u < NU - 1:
                    dve.wait_ge(down_done, at.chunk + NF)
                if u == U_A:
                    dve.wait_ge(pair_step, 5 * B)
                if u == U_L1:
                    dve.wait_ge(bias_loaded, 16 * (NQ + 3 * B))
                for k in range(DK):
                    if u == NU - 1:
                        dve.wait_ge(*[(last_half, 1), (down_done, NF * NU)][k])
                    ps = out_ps[u % 2][k][:, :]
                    b = t // TB
                    if u < U_A:
                        dst = share_out[:, m, t, k, :]
                        op = dve.tensor_copy(dst, ps)
                    elif u < U_B:
                        op = dve.tensor_scalar(mix_v[:, t, k, :], ps, pair_w[:, b, 0:1], None, ALU.mult)
                    elif u < U_L1:
                        op = dve.scalar_tensor_tensor(out=mix_v[:, t, k, :], in0=ps, scalar=pair_w[:, b, 1:2],
                                                      in1=mix_v[:, t, k, :], op0=ALU.mult, op1=ALU.add)
                    else:
                        x1 = share_out[:, 0, t, k, :]
                        op = dve.scalar_tensor_tensor(out=x1, in0=ps, scalar=b2[:, b, k:k + 1], in1=x1,
                                                      op0=ALU.add, op1=ALU.add)
                    if u == NU - 1 and k == 0:
                        op.then_inc(last_taken, 1)
                op.then_inc(out_taken, 1)

            def pair_bias_steps():
                dve.wait_ge(gv_loaded, 32 * B)
                for b in range(B):
                    dve.tensor_reduce(pair_max[:, b:b + 1], gv[:, b, 0:4], AX.X, ALU.max).then_inc(pair_step, 1)
                dve.wait_ge(pair_step, B)
                dve.tensor_scalar(pair_bias[:, :], pair_max[:, :], -SHARPNESS, None, ALU.mult).then_inc(pair_step, B)

            def pair_weight_steps():
                dve.wait_ge(pair_exp_done, B)
                for b in range(B):
                    dve.tensor_reduce(pair_sum[:, b:b + 1], pair_exp[:, b, 0:4], AX.X, ALU.add)\
                        .then_inc(pair_step, 1)
                dve.wait_ge(pair_step, 3 * B)
                dve.reciprocal(pair_inv[:, :], pair_sum[:, :]).then_inc(pair_step, B)
                dve.wait_ge(pair_step, 4 * B)
                for b in range(B):
                    dve.tensor_scalar(pair_w[:, b, :], pair_exp[:, b, 4:6], pair_inv[:, b:b + 1], None, ALU.mult)\
                        .then_inc(pair_step, 1)

            def gate_term(b, n):
                count = GATE_TERMS * b + gate_order.index(n)
                t, k = TB * b, n % DK
                col = mix_v[:, t, k, 0:1] if n < DK else share_out[:, n // DK - 1, t, k, 0:1]
                if count == 0:
                    dve.wait_ge(gw_loaded, 32)
                if n == gate_order[0]:
                    if b:
                        dve.wait_ge(gate_up, b)
                    op = dve.tensor_scalar(gate_part[:, :], gw1[:, n, :], col, None, ALU.mult)
                else:
                    dve.wait_ge(gate_sums, count)
                    if n == 0:
                        dve.wait_ge(out_taken, U_B + TB * b + 1)
                    op = dve.scalar_tensor_tensor(out=gate_part[:, :], in0=gw1[:, n, :], scalar=col,
                                                  in1=gate_part[:, :], op0=ALU.mult, op1=ALU.add)
                op.then_inc(gate_sums, 1)

            def gate_hidden(b):
                dve.wait_ge(gate_up, b + 1)
                for half in range(DK):
                    op = dve.tensor_scalar(gate_hid[:, half, :], zeros[:, :], out_ps[0][0][:, half:half + 1], 0.0,
                                           ALU.add, ALU.max)
                op.then_inc(gate_hid_done, 1)

            def gate_maximum(b):
                dve.wait_ge(gate_logits, b + 1)
                dve.tensor_reduce(gate_max[:, b:b + 1], out_ps[0][1][:, 0:4], AX.X, ALU.max).then_inc(gate_step, 1)
                dve.wait_ge(gate_step, GATE_STEPS * b + 1)
                dve.tensor_scalar(gate_bias[:, b:b + 1], gate_max[:, b:b + 1], -1.0, None, ALU.mult)\
                    .then_inc(gate_step, 1)

            def gate_softmax(b):
                dve.wait_ge(gate_exp_done, b + 1)
                dve.tensor_reduce(gate_sum[:, b:b + 1], gate_exp[:, b, :], AX.X, ALU.add).then_inc(gate_step, 1)
                dve.wait_ge(gate_step, GATE_STEPS * b + 3)
                dve.reciprocal(gate_inv[:, b:b + 1], gate_sum[:, b:b + 1]).then_inc(gate_step, 1)
                dve.wait_ge(gate_step, GATE_STEPS * b + 4)
                dve.tensor_scalar(gate[:, b, :], gate_exp[:, b, :], gate_inv[:, b:b + 1], None, ALU.mult)\
                    .then_inc(gate_step, 1)

            def mixture(n):
                kind, h, k = mix_ops[n]
                t, half = h // DK, h % DK
                x1 = share_out[:, 0, t, half, :]
                hi, lo = x_hi[:, t, half, :], x_lo[:, t, half, :]
                if kind == "lo":
                    dve.wait_ge(x1_hi_done, h + 1)
                    dve.tensor_tensor(lo, x1, hi.bitcast(f32), ALU.subtract).then_inc(x1_split, 1)
                    return
                g = gate[:, t // TB, :]
                if k == 0:
                    dve.wait_ge(gate_step, GATE_STEPS * (t // TB + 1))
                else:
                    dve.wait_ge(mix_step, mix_sums[n])
                if k == 4:
                    op = dve.tensor_tensor(x1, x1, lo.bitcast(f32), ALU.add)
                else:
                    a, w, c = [(x1, 1, hi.bitcast(f32)), (mix_v[:, t, half, :], 0, x1),
                               (share_out[:, 1, t, half, :], 2, x1), (share_out[:, 2, t, half, :], 3, x1)][k]
                    op = dve.scalar_tensor_tensor(out=x1, in0=a, scalar=g[:, w:w + 1], in1=c, op0=ALU.mult,
                                                  op1=ALU.add)
                op.then_inc(mix_step, 1)

            def unit(at, slot=None, m=None):
                u = at.i
                for f in range(NF):
                    if (u, f - 1) in X_STEPS:
                        x_half(X_STEPS[u, f - 1])
                    if (u, f) in X_STEPS:
                        x_turn(X_STEPS[u, f])
                    if u == TURN_UNIT:
                        turn_piece(f)
                    if u == ROWS_UNIT and f == 0:
                        dve.wait_ge(rows_loaded, 16 * NQ)
                        dve.transpose(rows_turned, rows_raw).then_inc(rows_done, 1)
                    for n in mix_plan.get((u, f), ()):
                        mixture(n)
                    if u in SPLITS and f:
                        split(at, slot, f - 1)
                    if (u, f) in gate_plan:
                        gate_term(*gate_plan[u, f])
                    if u in GATE_UNITS and f == 3:
                        gate_hidden(GATE_UNITS[u])
                    if u in GATE_UNITS and f == 5:
                        gate_maximum(GATE_UNITS[u])
                    if u in GATE_UNITS and f == 6:
                        gate_softmax(GATE_UNITS[u])
                    if u < U_L1 - 1 or u == U_L1 - 1 and f + 2 < NF:
                        relu_lo(at, f + 2)
                    elif NF * u + f + 2 < NF * NU:
                        gelu_split(NF * u + f + 2)
                    if u == 0 and f + 4 < NF:
                        first_set(f + 4)
                take_out(at, m)
                if u in SPLITS:
                    split(at, slot, NF - 1)

            x_half(0)
            first_set(0)
            x_half(1)
            for f in range(1, 3):
                first_set(f)
            relu_lo(fixed(0), 0)
            first_set(3)
            relu_lo(fixed(0), 1)
            for u in range(NT):
                unit(fixed(u), slot=1, m=0)
                if u == 1:
                    pair_bias_steps()
                if u == 3:
                    pair_weight_steps()
            for m, at in shared_loop(dve):
                unit(at, slot=m - 1, m=m)
            for u in range(U_A, NU):
                unit(fixed(u), slot=SPLITS.get(u, 0) % 2)


_INS = ['x', 'itok_B_0_2', 'itok_B_0_15', 'L0_cond_expert_wi', 'L0_cond_expert_wo', 'L0_cond_share_wi',
        'L0_cond_share_wo', 'L0_cond_gate_vecs', 'L0_cond_gate_w1', 'L0_cond_gate_w2', 'L1_cond_fc1_w',
        'L1_cond_fc1_b', 'L1_cond_fc2_w', 'L1_cond_fc2_b', 'L1_cond_experts_w', 'L1_cond_experts_b']


def kernel(**inputs):
    import numpy as _np
    import concourse.bacc as _bacc
    from concourse import mybir as _mybir
    from concourse.bass_utils import run_bass_kernel_spmd as _run

    nc = _bacc.Bacc("TRN2", target_bir_lowering=False, num_devices=1)
    arrays, args = {}, []
    for name in _INS:
        a = _np.ascontiguousarray(inputs[name])
        arrays[f"in_{name}_dram"] = a
        args.append(nc.dram_tensor(f"in_{name}_dram", a.shape, _mybir.dt.from_np(a.dtype), kind="ExternalInput").ap())
    x = inputs['x']
    args.append(nc.dram_tensor("out_0_dram", x.shape, _mybir.dt.float32, kind="ExternalOutput").ap())
    residual_moe_program(nc, *args)
    r = _run(nc, [arrays], core_ids=[0])
    return r.results[0]["out_0_dram"]
```
